# Optimizing a Trainium2 kernel written in Bass

```python
import numpy as np
import jax
import jax.numpy as jnp

def _softmax(x, axis=-1):
    return jax.nn.softmax(x, axis=axis)

def _gelu(x):
    return jax.nn.gelu(x, approximate=True)

def _silu(x):
    return jax.nn.silu(x)

def _sigmoid(x):
    return jax.nn.sigmoid(x)

def _layernorm(x, axis=-1, eps=1e-05):
    m = jnp.mean(x, axis=axis, keepdims=True)
    v = jnp.var(x, axis=axis, keepdims=True)
    return (x - m) / jnp.sqrt(v + eps)

def _scatter_add(tgt, idx, src, axis=0):
    return tgt.at[idx].add(src)

def _segment_sum(src, seg, n):
    return jax.ops.segment_sum(src, seg, n)
kernel_name = 'mk_decoder_postln_d1_seqx_r4_5d1401'

def setup_inputs(seed: int=0):
    np.random.seed(seed)
    _w = jnp.asarray

    def _rec_inputs():
        import jax
        import jax.numpy as jnp
        _rk = jax.random.key(seed)
        x = -0.0002928 + 1 * jax.random.normal(jax.random.fold_in(_rk, 1), (32, 112, 256), jnp.float32)
        _lenS = 112 - jax.random.randint(jax.random.fold_in(_rk, 7), (32,), 0, max(1, 112 // 4) + 1, jnp.int32)
        _lenS2 = 375 - jax.random.randint(jax.random.fold_in(_rk, 8), (32,), 0, max(1, 375 // 4) + 1, jnp.int32)
        _ctx_1024P = jax.random.normal(jax.random.fold_in(_rk, 11), (32, 16, 256), jnp.float32)
        _ctx_1024c = jax.random.dirichlet(jax.random.fold_in(_rk, 511), 0.3 * jnp.ones((16,), jnp.float32), (32, 375))
        _ctx_1024t = jnp.einsum('bsk,bkd->bsd', _ctx_1024c, _ctx_1024P)
        _ctx_1024t = _ctx_1024t * jax.lax.rsqrt(jnp.mean(jnp.square(_ctx_1024t)) + 1e-12) * 0.953939
        ctx_1024 = -1.39393e-06 + 0.999914 * (_ctx_1024t + 0.3 * jax.random.normal(jax.random.fold_in(_rk, 611), (32, 375, 256), jnp.float32))
        return (x, ctx_1024)
    x, ctx_1024 = _rec_inputs()

    def _L0_attn_setup():
        import jax, jax.numpy as jnp
        import numpy as np
        DIM = 256
        HEADS = 16
        HEAD_DIM = DIM // HEADS
        B, N = (2, 512)
        SCALE = 1.0 / np.float32(np.sqrt(DIM))

        def _split_heads(t):
            b, n, _ = t.shape
            return jnp.moveaxis(t.reshape(b, n, HEADS, HEAD_DIM), 2, 0)
        key = jax.random.key(seed)
        ks = jax.random.split(key, 9)
        s = 0.02
        return {'x': jax.random.normal(ks[0], (B, N, DIM), dtype=jnp.float32), 'Wq': jax.random.normal(ks[1], (DIM, DIM), dtype=jnp.float32) * s, 'bq': jax.random.normal(ks[2], (DIM,), dtype=jnp.float32) * s, 'Wk': jax.random.normal(ks[3], (DIM, DIM), dtype=jnp.float32) * s, 'bk': jax.random.normal(ks[4], (DIM,), dtype=jnp.float32) * s, 'Wv': jax.random.normal(ks[5], (DIM, DIM), dtype=jnp.float32) * s, 'bv': jax.random.normal(ks[6], (DIM,), dtype=jnp.float32) * s, 'Wo': jax.random.normal(ks[7], (DIM, DIM), dtype=jnp.float32) * s, 'bo': jax.random.normal(ks[8], (DIM,), dtype=jnp.float32) * s}
    _L0_attn_all = _L0_attn_setup()
    _L0_attn_in = {k: v for k, v in _L0_attn_all.items() if k in ('Wq', 'bq', 'Wk', 'bk', 'Wv', 'bv', 'Wo', 'bo')}
    del _L0_attn_all

    def _L0_xattn_setup():
        import jax, jax.numpy as jnp
        import numpy as np
        import math
        EMBED_DIM = 256
        NUM_HEADS = 16
        HEAD_DIM = EMBED_DIM // NUM_HEADS
        SUB_HEAD_DIM = HEAD_DIM // 2
        SCALING = 1.0 / math.sqrt(SUB_HEAD_DIM)
        LAMBDA_INIT = 0.8 - 0.6 * math.exp(-0.3 * 0)
        key = jax.random.key(seed)
        ks = jax.random.split(key, 10)
        B, T, D = (2, 512, EMBED_DIM)
        xav = math.sqrt(6.0 / (D + D))
        return {'query': jax.random.normal(ks[0], (B, T, D), jnp.float32), 'key': jax.random.normal(ks[1], (B, T, D), jnp.float32), 'value': jax.random.normal(ks[2], (B, T, D), jnp.float32), 'in_proj_weight': jax.random.uniform(ks[3], (3 * D, D), jnp.float32, -xav, xav), 'in_proj_bias': jnp.zeros((3 * D,), jnp.float32), 'out_proj_weight': jax.random.uniform(ks[4], (D, D), jnp.float32, -xav, xav), 'out_proj_bias': jnp.zeros((D,), jnp.float32), 'lambda_q1': 0.1 * jax.random.normal(ks[5], (SUB_HEAD_DIM,), jnp.float32), 'lambda_k1': 0.1 * jax.random.normal(ks[6], (SUB_HEAD_DIM,), jnp.float32), 'lambda_q2': 0.1 * jax.random.normal(ks[7], (SUB_HEAD_DIM,), jnp.float32), 'lambda_k2': 0.1 * jax.random.normal(ks[8], (SUB_HEAD_DIM,), jnp.float32)}
    _L0_xattn_all = _L0_xattn_setup()
    _L0_xattn_in = {k: v for k, v in _L0_xattn_all.items() if k in ('in_proj_weight', 'in_proj_bias', 'out_proj_weight', 'out_proj_bias', 'lambda_q1', 'lambda_k1', 'lambda_q2', 'lambda_k2')}
    del _L0_xattn_all

    def _L0_ffn_setup():
        import jax, jax.numpy as jnp
        import numpy as np
        B, S, H = (4, 512, 256)
        F = 1024
        E = 8
        JITTER_EPS = 0.01

        def _sparse_mixer_top2(scores, jitter_eps):
            vals, idx = jax.lax.top_k(scores, 2)
            neg_inf = -jnp.inf
            m1 = vals[:, :1]
            factor1 = jnp.maximum(jnp.abs(scores), m1)
            mask1 = (m1 - scores) / factor1 > 2 * jitter_eps
            p1 = jax.nn.softmax(jnp.where(mask1, neg_inf, scores), axis=-1)
            mult1 = jnp.take_along_axis(p1, idx[:, :1], axis=-1)[:, 0]
            m2 = vals[:, 1:2]
            factor2 = jnp.maximum(jnp.abs(scores), m2)
            mask2 = (m2 - scores) / factor2 > 2 * jitter_eps
            top1_onehot = jnp.arange(scores.shape[-1])[None, :] == idx[:, :1]
            s2 = jnp.where(top1_onehot, neg_inf, scores)
            p2 = jax.nn.softmax(jnp.where(mask2, neg_inf, s2), axis=-1)
            mult2 = jnp.take_along_axis(p2, idx[:, 1:2], axis=-1)[:, 0]
            return (mult1, mult2, idx)
        key = jax.random.key(seed)
        k0, k1, k2, k3, k4 = jax.random.split(key, 5)
        hidden_states = jax.random.normal(k0, (B, S, H), dtype=jnp.float32)
        gate_w = jax.random.normal(k1, (E, H), dtype=jnp.float32) * 0.02
        w1 = jax.random.normal(k2, (E, F, H), dtype=jnp.float32) * 0.02
        w2 = jax.random.normal(k3, (E, H, F), dtype=jnp.float32) * 0.02
        w3 = jax.random.normal(k4, (E, F, H), dtype=jnp.float32) * 0.02
        return {'hidden_states': hidden_states, 'gate_w': gate_w, 'w1': w1, 'w2': w2, 'w3': w3}
    _L0_ffn_all = _L0_ffn_setup()
    _L0_ffn_in = {k: v for k, v in _L0_ffn_all.items() if k in ('gate_w', 'w1', 'w2', 'w3')}
    del _L0_ffn_all
    return {'x': x, 'ctx_1024': ctx_1024, 'L0_attn_Wq': _L0_attn_in['Wq'], 'L0_attn_bq': _L0_attn_in['bq'], 'L0_attn_Wk': _L0_attn_in['Wk'], 'L0_attn_bk': _L0_attn_in['bk'], 'L0_attn_Wv': _L0_attn_in['Wv'], 'L0_attn_bv': _L0_attn_in['bv'], 'L0_attn_Wo': _L0_attn_in['Wo'], 'L0_attn_bo': _L0_attn_in['bo'], 'L0_xattn_in_proj_weight': _L0_xattn_in['in_proj_weight'], 'L0_xattn_in_proj_bias': _L0_xattn_in['in_proj_bias'], 'L0_xattn_out_proj_weight': _L0_xattn_in['out_proj_weight'], 'L0_xattn_out_proj_bias': _L0_xattn_in['out_proj_bias'], 'L0_xattn_lambda_q1': _L0_xattn_in['lambda_q1'], 'L0_xattn_lambda_k1': _L0_xattn_in['lambda_k1'], 'L0_xattn_lambda_q2': _L0_xattn_in['lambda_q2'], 'L0_xattn_lambda_k2': _L0_xattn_in['lambda_k2'], 'L0_ffn_gate_w': _L0_ffn_in['gate_w'], 'L0_ffn_w1': _L0_ffn_in['w1'], 'L0_ffn_w2': _L0_ffn_in['w2'], 'L0_ffn_w3': _L0_ffn_in['w3']}

def reference(x, ctx_1024, L0_attn_Wq, L0_attn_bq, L0_attn_Wk, L0_attn_bk, L0_attn_Wv, L0_attn_bv, L0_attn_Wo, L0_attn_bo, L0_xattn_in_proj_weight, L0_xattn_in_proj_bias, L0_xattn_out_proj_weight, L0_xattn_out_proj_bias, L0_xattn_lambda_q1, L0_xattn_lambda_k1, L0_xattn_lambda_q2, L0_xattn_lambda_k2, L0_ffn_gate_w, L0_ffn_w1, L0_ffn_w2, L0_ffn_w3):
    import jax
    import jax.numpy as jnp

    def _L0_attn_ref(x, Wq, bq, Wk, bk, Wv, bv, Wo, bo):
        import jax, jax.numpy as jnp
        import numpy as np
        DIM = 256
        HEADS = 16
        HEAD_DIM = DIM // HEADS
        B, N = (2, 512)
        SCALE = 1.0 / np.float32(np.sqrt(DIM))

        def _split_heads(t):
            b, n, _ = t.shape
            return jnp.moveaxis(t.reshape(b, n, HEADS, HEAD_DIM), 2, 0)
        q = _split_heads(x @ Wq.T + bq)
        k = _split_heads(x @ Wk.T + bk)
        v = _split_heads(x @ Wv.T + bv)
        scores = jnp.einsum('hbnd,hbmd->hbnm', k, q) * SCALE
        attn = jax.nn.softmax(scores, axis=-1)
        out = jnp.einsum('hbnm,hbmd->hbnd', attn, v)
        out = jnp.moveaxis(out, 0, 2).reshape(x.shape[0], x.shape[1], DIM)
        return out @ Wo.T + bo

    def _L0_xattn_ref(query, key, value, in_proj_weight, in_proj_bias, out_proj_weight, out_proj_bias, lambda_q1, lambda_k1, lambda_q2, lambda_k2):
        import jax, jax.numpy as jnp
        import numpy as np
        import math
        EMBED_DIM = 256
        NUM_HEADS = 16
        HEAD_DIM = EMBED_DIM // NUM_HEADS
        SUB_HEAD_DIM = HEAD_DIM // 2
        SCALING = 1.0 / math.sqrt(SUB_HEAD_DIM)
        LAMBDA_INIT = 0.8 - 0.6 * math.exp(-0.3 * 0)
        B, T, D = query.shape
        S = key.shape[1]
        H, hd, sd = (NUM_HEADS, HEAD_DIM, SUB_HEAD_DIM)
        qw, kw, vw = jnp.split(in_proj_weight, 3, axis=0)
        qb, kb, vb = jnp.split(in_proj_bias, 3, axis=0)
        q = query @ qw.T + qb
        k = key @ kw.T + kb
        v = value @ vw.T + vb
        q = q.reshape(B, T, H, hd).transpose(0, 2, 1, 3)
        k = k.reshape(B, S, H, hd).transpose(0, 2, 1, 3)
        v = v.reshape(B, S, H, hd).transpose(0, 2, 1, 3)
        q1, q2 = (q[..., :sd], q[..., sd:])
        k1, k2 = (k[..., :sd], k[..., sd:])
        logits_1 = jnp.einsum('bhtd,bhsd->bhts', q1, k1) * SCALING
        logits_2 = jnp.einsum('bhtd,bhsd->bhts', q2, k2) * SCALING
        a1 = jax.nn.softmax(logits_1, axis=-1)
        a2 = jax.nn.softmax(logits_2, axis=-1)
        lam = jnp.exp(jnp.dot(lambda_q1, lambda_k1)) - jnp.exp(jnp.dot(lambda_q2, lambda_k2)) + LAMBDA_INIT
        diff_weights = a1 - lam * a2
        attn_output = jnp.einsum('bhts,bhsd->bhtd', diff_weights, v)
        attn_output = attn_output * (1.0 - LAMBDA_INIT)
        attn_output = attn_output.transpose(0, 2, 1, 3).reshape(B, T, D)
        output = attn_output @ out_proj_weight.T + out_proj_bias
        return output

    def _L0_ffn_ref(hidden_states, gate_w, w1, w2, w3):
        import jax, jax.numpy as jnp
        import numpy as np
        B, S, H = (4, 512, 256)
        F = 1024
        E = 8
        JITTER_EPS = 0.01

        def _sparse_mixer_top2(scores, jitter_eps):
            vals, idx = jax.lax.top_k(scores, 2)
            neg_inf = -jnp.inf
            m1 = vals[:, :1]
            factor1 = jnp.maximum(jnp.abs(scores), m1)
            mask1 = (m1 - scores) / factor1 > 2 * jitter_eps
            p1 = jax.nn.softmax(jnp.where(mask1, neg_inf, scores), axis=-1)
            mult1 = jnp.take_along_axis(p1, idx[:, :1], axis=-1)[:, 0]
            m2 = vals[:, 1:2]
            factor2 = jnp.maximum(jnp.abs(scores), m2)
            mask2 = (m2 - scores) / factor2 > 2 * jitter_eps
            top1_onehot = jnp.arange(scores.shape[-1])[None, :] == idx[:, :1]
            s2 = jnp.where(top1_onehot, neg_inf, scores)
            p2 = jax.nn.softmax(jnp.where(mask2, neg_inf, s2), axis=-1)
            mult2 = jnp.take_along_axis(p2, idx[:, 1:2], axis=-1)[:, 0]
            return (mult1, mult2, idx)
        Bv, Sv, Hv = hidden_states.shape
        x = hidden_states.reshape(-1, Hv)
        scores = x @ gate_w.T
        mult1, mult2, idx = _sparse_mixer_top2(scores, JITTER_EPS)
        out = jnp.zeros_like(x)
        for e in range(E):
            w_tok = mult1 * (idx[:, 0] == e) + mult2 * (idx[:, 1] == e)
            h = jax.nn.silu(x @ w1[e].T) * (x @ w3[e].T)
            out = out + w_tok[:, None] * (h @ w2[e].T)
        return out.reshape(Bv, Sv, Hv)
    x = _layernorm(x + _L0_attn_ref(x, L0_attn_Wq, L0_attn_bq, L0_attn_Wk, L0_attn_bk, L0_attn_Wv, L0_attn_bv, L0_attn_Wo, L0_attn_bo), axis=-1)
    x = _layernorm(x + _L0_xattn_ref(x, ctx_1024, ctx_1024, L0_xattn_in_proj_weight, L0_xattn_in_proj_bias, L0_xattn_out_proj_weight, L0_xattn_out_proj_bias, L0_xattn_lambda_q1, L0_xattn_lambda_k1, L0_xattn_lambda_q2, L0_xattn_lambda_k2), axis=-1)
    x = _layernorm(x + _L0_ffn_ref(x, L0_ffn_gate_w, L0_ffn_w1, L0_ffn_w2, L0_ffn_w3), axis=-1)
    return x

_drawn_inputs = setup_inputs


def setup_inputs(seed=0):
    import zlib

    import numpy as np

    out = dict(_drawn_inputs(seed))
    spreads = {'L0_xattn_in_proj_bias': (0.0, 0.1), 'L0_xattn_out_proj_bias': (0.0, 0.1)}
    factors = {'L0_attn_Wq': 8.0,
     'L0_attn_bq': 8.0,
     'L0_attn_Wk': 8.0,
     'L0_attn_bk': 8.0,
     'L0_attn_Wv': 5.615,
     'L0_attn_bv': 7.97,
     'L0_attn_Wo': 4.728,
     'L0_attn_bo': 2.932,
     'L0_xattn_lambda_q1': 7.988,
     'L0_xattn_lambda_k1': 4.888,
     'L0_xattn_lambda_q2': 2.943,
     'L0_xattn_lambda_k2': 2.68}
    for name, (base, spread) in spreads.items():
        noise = np.random.default_rng([zlib.crc32(name.encode()), seed]).standard_normal(out[name].shape)
        drawn = base * np.exp(spread * noise) if base else spread * noise
        out[name] = jnp.asarray(drawn.astype(out[name].dtype))
    for name, factor in factors.items():
        out[name] = (out[name] * factor).astype(out[name].dtype)
    return out
```

```python
from contextlib import ExitStack

import concourse.bass as bass
from concourse import mybir

F32 = mybir.dt.float32
F16 = mybir.dt.float16
I32 = mybir.dt.int32
ACT = mybir.ActivationFunctionType
ALU = mybir.AluOpType
AX = mybir.AxisListType

B, T, D = 32, 112, 256
S, SC = 375, 125
H, DH = 16, 16
KD = D // 128
NT = B * T
EXP, FF = 8, 1024
LAMBDA_INIT = 0.2
EPS = 1e-5
VW = DH + 1
VROW = H * VW
TERMS = 3
STACK = TERMS * 32
PAIRS = H // 2
WSCALE = 64.0
WCOLS = 2 * KD * FF + FF // 128 * D
CUTS = B // EXP
CUT = WCOLS // CUTS


class Phase:

    def __init__(self, nc, ctx, name):
        self.nc, self.ctx, self.name, self.semaphores = nc, ctx, name, []
        ctx.callback(self.close)

    def close(self):
        self.nc.clear_and_free_semaphores(self.semaphores)
        self.nc.all_engine_barrier()

    def sb(self, name, shape, dt):
        return self.ctx.enter_context(self.nc.sbuf_tensor(f"{self.name}_{name}", shape, dt))

    def ps(self, name, shape, dt=F32):
        return self.ctx.enter_context(self.nc.psum_tensor(f"{self.name}_{name}", shape, dt))

    def sem(self, name):
        self.semaphores.append(self.nc.alloc_semaphore(f"{self.name}_{name}"))
        return self.semaphores[-1]

    def sems(self, name, n):
        return [self.sem(f"{name}{i}") for i in range(n)]


class Step:

    def __init__(self, m, c, unroll, count):
        self.m, self.c, self.unroll, self.n = m, c, unroll, count

    def live(self, lag=0):
        return self.m is not None or 0 <= self.c + lag < self.n

    def item(self, lag=0):
        return self.c + lag if self.m is None else self.m * self.unroll + (self.c + lag)

    def slot(self, lag=0):
        return (self.c + lag) % self.unroll

    def uses(self, lag=0):
        n = (self.c + lag) // self.unroll + 1
        return n if self.m is None else self.m + n

    def count(self, per, lag=0, off=None):
        off = per if off is None else off
        if self.m is None:
            item = self.c + lag
            return per * self.n if item >= self.n else per * item + off
        return self.m * (self.unroll * per) + (per * (self.c + lag) + off)


def wait_alone(eng, sem, value, holds):
    eng.wait_ge(*holds)
    wait(eng, sem, value)


def wait(eng, sem, value):
    if not isinstance(value, int) or value > 0:
        eng.wait_ge(sem, value)


def pipeline(eng, body, count, unroll, first, lead, lag):
    loops = (count - lead - first) // unroll
    for c in range(-lead, first):
        body(Step(None, c, unroll, count))
    with eng.Fori(0, loops) as m:
        for c in range(first, first + unroll):
            body(Step(m, c, unroll, count))
    for c in range(first + loops * unroll, count + lag):
        body(Step(None, c, unroll, count))


def project(nc, name, src, chunks, width, transposed, values, rows):
    nw = len(transposed) + 1
    tiles = width // rows
    tb = KD * len(transposed)
    banks = tb + tiles
    with ExitStack() as ctx:
        ph = Phase(nc, ctx, name)
        w = ph.sb("w", [128, nw, KD, D], F32)
        w_hi = ph.sb("w_hi", [128, nw, KD, D], F16)
        w_lo = ph.sb("w_lo", [128, nw, KD, D], F16)
        bias_t = ph.sb("bias_t", [128, len(transposed), KD], F32)
        bias_v = ph.sb("bias_v", [128, D], F32)
        x = ph.sb("x", [128, 2, KD, width], F32)
        x_hi = ph.sb("x_hi", [128, 2, KD, width], F16)
        x_lo = ph.sb("x_lo", [128, 2, KD, width], F16)
        t_hi = ph.sb("t_hi", [128, 2, tb, width], F16)
        t_lo = ph.sb("t_lo", [128, 2, tb, width], F16)
        v = ph.sb("v", [128, 2, tiles, VROW], F32)
        bank = [ph.ps(f"bank{i}", [128, 512]) for i in range(banks)]
        w_loaded, w_hi_ready, w_ready, ones_ready = (ph.sem(s) for s in
                                                     ("w_loaded", "w_hi_ready", "w_ready", "ones_ready"))
        x_loaded = ph.sems("x_loaded", 2)
        stored = ph.sems("stored", 2)
        x_hi_ready, x_ready, bank_full, t_hi_ready, bank_empty = (
            ph.sem(s) for s in ("x_hi_ready", "x_ready", "bank_full", "t_hi_ready", "bank_empty"))
        w_dmas = nw + len(transposed) + 1
        stores = sum(len(t[2]) for t in transposed) + 1
        src_v = src.rearrange("(k p) n -> p k n", p=128)
        out_v = values[2].rearrange("(c j p) n -> p c j n", c=chunks, p=rows)

        with nc.Block() as block:

            @block.sync
            def _(sp):
                for i, t in enumerate(transposed):
                    sp.dma_start(w[:, i], t[0].rearrange("(k p) n -> p k n", p=128)).then_inc(w_loaded, 16)
                    sp.dma_start(bias_t[:, i], t[1]).then_inc(w_loaded, 16)
                sp.dma_start(w[:, nw - 1], values[0].rearrange("(k p) n -> p k n", p=128)).then_inc(w_loaded, 16)
                sp.dma_start(bias_v[:], values[1][None, :].to_broadcast([128, D])).then_inc(w_loaded, 16)

                def load(s, lag):
                    if s.live(lag):
                        wait(sp, x_ready, s.count(1, lag - 2))
                        sp.dma_start(x[:, s.slot(lag)], src_v[:, :, bass.ts(s.item(lag), width)]).then_inc(
                            x_loaded[s.slot(lag)], 16)

                def body(s):
                    load(s, 2)
                    if not s.live():
                        return
                    p = s.slot()
                    wait(sp, bank_empty, s.count(banks))
                    for i, t in enumerate(transposed):
                        for half, out in t[2]:
                            sp.dma_start(out.rearrange("m p n -> p m n")[:, :, bass.ts(s.item(), width)],
                                         (t_hi, t_lo)[half][:, p, KD * i:KD * i + KD]).then_inc(stored[p], 16)
                    sp.dma_start(out_v[:, s.item()], v[0:rows, p]).then_inc(stored[p], 16)

                pipeline(sp, body, chunks, 2, 2, 2, 0)
                for p in range(2):
                    sp.wait_ge(stored[p], 16 * stores * (chunks // 2))

            @block.gpsimd
            def _(pool):
                for p in range(2):
                    pool.memset(v[:, p].rearrange("p j (h w) -> p (j h) w", w=VW)[:, :, DH:VW], 1.0).then_inc(ones_ready, 1)

            @block.scalar
            def _(act):
                act.wait_ge(w_loaded, 16 * w_dmas)
                nc.scalar.activation(w_hi[:], w[:], ACT.Copy).then_inc(w_hi_ready, 1)

                def body(s):
                    if s.live(1):
                        p = s.slot(1)
                        wait(act, x_loaded[p], s.uses(1) * 16)
                        wait(act, bank_full, s.count(banks, -1))
                        nc.scalar.activation(x_hi[:, p], x[:, p], ACT.Copy).then_inc(x_hi_ready, 1)
                    if not s.live():
                        return
                    p = s.slot()
                    wait(act, stored[p], (s.uses() - 1) * (16 * stores))
                    for j in range(tb):
                        i, m = divmod(j, KD)
                        wait(act, bank_full, s.count(banks, 0, j + 1))
                        nc.scalar.activation(t_hi[:, p, j], bank[j][:, 0:width], ACT.Identity,
                                             bias=bias_t[:, i, m:m + 1]).then_inc(t_hi_ready, 1)

                pipeline(act, body, chunks, 2, 2, 2, 0)

            @block.vector
            def _(dve):
                dve.wait_ge(w_hi_ready, 1)
                nc.vector.tensor_tensor(w_lo[:], w[:], w_hi[:], ALU.subtract).then_inc(w_ready, 1)
                dve.wait_ge(ones_ready, 2)

                def body(s):
                    if s.live(1):
                        p = s.slot(1)
                        wait(dve, x_hi_ready, s.count(1, 1))
                        wait(dve, bank_full, s.count(banks, -1))
                        nc.vector.tensor_tensor(x_lo[:, p], x[:, p], x_hi[:, p], ALU.subtract).then_inc(x_ready, 1)
                    if not s.live():
                        return
                    p = s.slot()
                    wait(dve, stored[p], (s.uses() - 1) * (16 * stores))
                    for j in range(tb):
                        i, m = divmod(j, KD)
                        wait(dve, t_hi_ready, s.count(tb, 0, j + 1))
                        nc.vector.scalar_tensor_tensor(
                            out=t_lo[:, p, j], in0=bank[j][:, 0:width], scalar=bias_t[:, i, m:m + 1],
                            in1=t_hi[:, p, j], op0=ALU.add, op1=ALU.subtract).then_inc(bank_empty, 1)
                    for j in range(tiles):
                        wait(dve, bank_full, s.count(banks, 0, tb + j + 1))
                        nc.vector.tensor_tensor(
                            v[0:rows, p, j].rearrange("p (h w) -> p h w", w=VW)[:, :, 0:DH],
                            bank[tb + j][0:rows, 0:D].rearrange("p (h w) -> p h w", w=DH),
                            bias_v[0:rows, :].rearrange("p (h w) -> p h w", w=DH), ALU.add).then_inc(bank_empty, 1)

                pipeline(dve, body, chunks, 2, 2, 2, 0)

            @block.tensor
            def _(pe):
                pe.wait_ge(w_ready, 1)

                def body(s):
                    if not s.live():
                        return
                    p = s.slot()
                    wait(pe, x_ready, s.count(1))
                    for j in range(banks):
                        wait(pe, bank_empty, s.count(banks, -1, j + 1))
                        terms = [(k, wt, xt) for k in range(KD) for wt, xt in ((w_hi, x_hi), (w_lo, x_hi), (w_hi, x_lo))]
                        for n, (k, wt, xt) in enumerate(terms):
                            flags = dict(start=n == 0, stop=n == len(terms) - 1)
                            if j < tb:
                                i, m = divmod(j, KD)
                                last = nc.tensor.matmul(bank[j][:, 0:width], wt[:, i, k, 128 * m:128 * m + 128],
                                                        xt[:, p, k], **flags)
                            else:
                                r = (j - tb) * rows
                                last = nc.tensor.matmul(bank[j][0:rows, 0:D], xt[:, p, k, r:r + rows],
                                                        wt[:, nw - 1, k, :], **flags)
                        last.then_inc(bank_full, 1)

                pipeline(pe, body, chunks, 2, 2, 2, 0)


class Shape:

    def __init__(self, name, units, chunks, rows, lead, scale):
        self.name, self.units, self.chunks, self.rows, self.lead, self.scale = name, units, chunks, rows, lead, scale
        self.per_pair = units // PAIRS
        self.unit_rows = 32 // self.per_pair
        self.keys = chunks * rows
        self.groups = units // 4
        self.parts = self.groups * chunks
        self.buffers = lead + 2
        self.halves = units // 16
        self.max_banks = 4 if self.keys > T else 1
        self.lag = self.chunks // 3 + 1


SELF = Shape("self", H, 1, T, 2, 1.0 / D ** 0.5)
CROSS = Shape("cross", 2 * H, S // SC, SC, 1, 1.0 / (DH // 2) ** 0.5)
PROBS = 4

SELF_STEPS = {"turn": (1, -4), "row0": (1, 1), "heads": (2, -2), "query": (2, -4), "out0": (3, -1), "proj": (3, -2)}
SELF_READS = {"turn": (1, -4), "row0": (1, 1), "heads": (2, -2), "query": (2, -4), "out0": (0, -2), "proj": (0, -3)}
CROSS_STEPS = {"row1": (0, 0), "out1": (4, -1), "heads": (7, -1), "proj": (9, -1),
               "out0": (16, 0), "row0": (18, 1), "turn": (20, -1), "score": (22, -1)}
CROSS_READS = {"row1": (0, 0), "out1": (5, -1), "heads": (8, -1), "proj": (10, -1),
               "out0": (17, 0), "row0": (18, 1), "turn": (21, -1), "score": (23, -1)}


def attention(nc, sh, key, query, value, resid, wo, bo, x_out, wq=None, bq=None, q_out=None,
              w_in=None, w_out16=None, gate=None, score_out=None, lambdas=None):
    is_self = sh is SELF
    steps, reads = (SELF_STEPS, SELF_READS) if is_self else (CROSS_STEPS, CROSS_READS)
    nb, parts, groups, chunks, rows, lead = sh.buffers, sh.parts, sh.groups, sh.chunks, sh.rows, sh.lead
    pairs_of = (lambda g: [2 * g, 2 * g + 1]) if is_self else (lambda g: [g])
    head_of = (lambda g, i: 4 * g + i) if is_self else (lambda g, i: 2 * g + i // 2)
    pair_w = sh.per_pair * T
    loads = 1 + sh.per_pair + 1 if is_self else TERMS * (1 + sh.per_pair) + 1
    first_evac, last_evac = (1, 1) if is_self else (14, 2)
    ln_lag = reads["proj"][1]
    aggregate_part, norm_part = (1, 2) if is_self else (11, 16)
    max_lag = max(-lag for _, lag in list(steps.values()) + list(reads.values()))
    names = list(steps)
    max_banks, step_banks = (2, 2) if is_self else (3, 1)

    with ExitStack() as ctx:
        ph = Phase(nc, ctx, sh.name)
        ident = ph.sb("ident", [128, 128], F32)
        w_out = ph.sb("w_out", [128, KD, D], F32)
        b_out = ph.sb("b_out", [T, D], F32)
        kst = ph.sb("kst", [STACK + 1, nb, PAIRS, sh.keys], F16)
        qst = ph.sb("qst", [STACK + 1, nb, PAIRS, pair_w], F16)
        val = ph.sb("val", [rows, nb, chunks * VROW + 16], F32)
        mx = ph.sb("mx", [T, nb, sh.units], F32)
        neg_mx = ph.sb("neg_mx", [16, nb, sh.halves, T], F16)
        probs = ph.sb("probs", [rows, PROBS, 4 * T], F32)
        outs = ph.sb("outs", [128, 2, 4 * T], F32)
        recip = ph.sb("recip", [T, nb, sh.units], F32)
        weight = ph.sb("weight", [T, nb, sh.units], F32)
        prod = ph.sb("prod", [T, nb, 16, DH], F32)
        heads = ph.sb("heads", [T, nb, D], F32)
        heads_t = ph.sb("heads_t", [128, nb, KD, T], F32)
        x_in = ph.sb("x_in", [T, nb, D], F32)
        x_bias = ph.sb("x_bias", [T, nb, D], F32)
        r = ph.sb("r", [T, nb, D], F32)
        stats = ph.sb("stats", [T, nb, 6], F32)
        mv = ph.sb("mv", [T, nb, 2], F32)
        small = ph.sb("small", [T, nb, 4], F32)
        power = ph.sb("power", [T, 3], F32)
        y = ph.sb("y", [T, nb, D], F32)
        if is_self:
            wq_f = ph.sb("wq_f", [128, KD, D], F32)
            wq_hi = ph.sb("wq_hi", [128, KD, D], F16)
            wq_lo = ph.sb("wq_lo", [128, KD, D], F16)
            bq_t = ph.sb("bq_t", [128, KD], F32)
            y_hi = ph.sb("y_hi", [128, nb, KD, T], F16)
            y_lo = ph.sb("y_lo", [128, nb, KD, T], F16)
            q_hi = ph.sb("q_hi", [128, nb, KD, T], F16)
            q_lo = ph.sb("q_lo", [128, nb, KD, T], F16)
            ew = ph.sb("ew", [128, 2, CUT], F32)
            ew_half = ph.sb("ew_half", [128, 2, 2, CUT], F16)
        else:
            gate_w = ph.sb("gate_w", [128, KD, EXP], F32)
            y_t = ph.sb("y_t", [128, nb, KD, T], F32)
            score = ph.sb("score", [T, nb, EXP], F32)
            lam_in = ph.sb("lam_in", [T, 4, DH // 2], F32)
            lam = ph.sb("lam", [T, 8], F32)
            lam_prod = ph.sb("lam_prod", [T, 2, DH // 2], F32)
            coef = ph.sb("coef", [T, 8, 2], F32)
        bank_max = [ph.ps(f"bank_max{i}", [128, 512]) for i in range(max_banks)]
        bank_score = [ph.ps(f"bank_score{i}", [128, 512]) for i in range(2)]
        bank_out = [ph.ps(f"bank_out{i}", [128, 512]) for i in range(2)]
        bank_step = [ph.ps(f"bank_step{i}", [128, 512]) for i in range(step_banks)]

        consts_loaded, wq_hi_ready, consts_ready, ident_ready, stacks_ready = (ph.sem(s) for s in (
            "consts_loaded", "wq_hi_ready", "consts_ready", "ident_ready", "stacks_ready"))
        lam_ready = ph.sem("lam_ready")
        loaded = ph.sems("loaded", nb)
        x_loaded = ph.sems("x_loaded", nb)
        row_loaded = [ph.sems(f"row_loaded{h}_", nb) for h in range(sh.halves)]
        x_stored = ph.sems("x_stored", nb)
        side_stored = ph.sems("side_stored", nb)
        max_full, max_read, scores_full, probs_ready, probs_used = (ph.sem(s) for s in (
            "max_full", "max_read", "scores_full", "probs_ready", "probs_used"))
        out_read = ph.sems("out_read", sh.halves)
        full = {n: ph.sem(f"full_{n}") for n in steps}
        read = {n: ph.sem(f"read_{n}") for n in steps}
        recip_ready, weight_ready, prod_ready, heads_ready, stats_ready, mv_ready = (
            ph.sem(s) for s in ("recip_ready", "weight_ready", "prod_ready", "heads_ready",
                                "stats_ready", "mv_ready"))
        x_bias_ready, small_ready, y_ready = (ph.sem(s) for s in ("x_bias_ready", "small_ready", "y_ready"))
        y_hi_ready, q_hi_ready = ph.sem("y_hi_ready"), ph.sem("q_hi_ready")
        ew_loaded, ew_stored = ph.sems("ew_loaded", 2), ph.sems("ew_stored", 2)
        ew_hi_ready, ew_ready = ph.sem("ew_hi_ready"), ph.sem("ew_ready")
        piece = CUT // parts
        consts = 2 + (2 if is_self else 5)
        side_stores = 2 if is_self else 1

        def bank_of(name):
            return bank_step[names.index(name) % step_banks]

        def max_bank(p, i):
            return bank_max[(p * 4 * groups + i) % max_banks]

        def run(eng, body):
            pipeline(eng, body, B, nb, nb + max_lag, lead + 1, max_lag)

        def loaded_value(s, lag):
            return s.uses(lag) * (16 * loads)

        with nc.Block() as block:

            @block.sync
            def _(sp):
                sp.dma_start(w_out[:], wo.rearrange("(k p) n -> p k n", p=128)).then_inc(consts_loaded, 16)
                sp.dma_start(b_out[:], bo[None, :].to_broadcast([T, D])).then_inc(consts_loaded, 16)
                if is_self:
                    sp.dma_start(wq_f[:], wq.rearrange("(k p) n -> p k n", p=128)).then_inc(consts_loaded, 16)
                    sp.dma_start(bq_t[:], bq).then_inc(consts_loaded, 16)
                else:
                    sp.dma_start(gate_w[:], gate.rearrange("(k p) n -> p k n", p=128)).then_inc(consts_loaded, 16)
                    for i, vec in enumerate(lambdas):
                        sp.dma_start(lam_in[:, i], vec[None, :].to_broadcast([T, DH // 2])).then_inc(consts_loaded, 16)
                sp.wait_ge(stacks_ready, 1)
                sp.wait_ge(ident_ready, 2)

                def load(s):
                    lag = lead + 1
                    if not s.live(lag):
                        return
                    p, b = s.slot(lag), s.item(lag)
                    keys = bass.ts(b, sh.keys)
                    wait(sp, scores_full, s.count(parts, lag - nb))
                    wait(sp, probs_used, s.count(parts, lag - nb))
                    if is_self:
                        sp.dma_start(kst[0:STACK, p], key.rearrange("(q g) n -> q g n", g=PAIRS)[:, :, keys]).then_inc(loaded[p], 16)
                        unit = STACK // sh.per_pair
                        for i in range(sh.per_pair):
                            sp.dma_start(qst[unit * i:unit * (i + 1), p, :, i * T:(i + 1) * T],
                                         query.rearrange("(q g) n -> q g n", g=PAIRS)[unit * i:unit * (i + 1), :, keys]
                                         ).then_inc(loaded[p], 16)
                    for term, half in () if is_self else enumerate((0, 1, 0)):
                        sp.dma_start(kst[32 * term:32 * term + 32, p],
                                     key[half].rearrange("(g r) n -> r g n", r=32)[:, :, keys]).then_inc(loaded[p], 16)
                    for term, half in () if is_self else enumerate((0, 0, 1)):
                        src = query[half].rearrange("(g i r) n -> i r g n", i=sh.per_pair, r=sh.unit_rows)
                        for i in range(sh.per_pair):
                            row = 32 * term + sh.unit_rows * i
                            sp.dma_start(qst[row:row + sh.unit_rows, p, :, i * T:(i + 1) * T],
                                         src[i, :, :, bass.ts(b, T)]).then_inc(loaded[p], 16)
                    sp.dma_start(val[:, p, 0:chunks * VROW].rearrange("p (c n) -> p c n", c=chunks),
                                 value.rearrange("(b c p) n -> p b c n", c=chunks, p=rows)[:, b]).then_inc(loaded[p], 16)
                    wait(sp, x_bias_ready, s.count(1, lag - nb))
                    sp.dma_start(x_in[:, p], resid[bass.ts(b, T), :]).then_inc(x_loaded[p], 16)

                def row(s, h):
                    name = f"row{h}"
                    lag = reads[name][1]
                    if not s.live(lag):
                        return
                    p = s.slot(lag)
                    wait(sp, read[name], s.count(1, lag))
                    n = 16 // sh.per_pair
                    sp.dma_start(qst[STACK:STACK + 1, p, h * n:h * n + n, :].rearrange("o g (i t) -> o (g i) t", t=T),
                                 neg_mx[:, p, h]).then_inc(row_loaded[h][p], 16)

                def weights(s):
                    if s.live(-1):
                        e = s.slot(-1) % 2
                        wait_alone(sp, ew_ready, s.count(parts, -1), (stacks_ready, 1))
                        sp.dma_start(w_out16[s.item(-1)], ew_half[:, e]).then_inc(ew_stored[e], 16)
                    if s.live(1):
                        e = s.slot(1) % 2
                        sp.dma_start(ew[:, e], w_in[s.item(1)]).then_inc(ew_loaded[e], 16)

                def body(s):
                    if is_self:
                        weights(s)
                    else:
                        row(s, 1)
                    load(s)
                    if is_self:
                        row(s, 0)
                    if s.live(ln_lag):
                        p = s.slot(ln_lag)
                        wait(sp, y_ready, s.count(1, ln_lag))
                        sp.dma_start(x_out[bass.ts(s.item(ln_lag), T), 0:D], y[:, p]).then_inc(x_stored[p], 16)
                    if is_self and s.live(steps["query"][1]):
                        lag = steps["query"][1]
                        p = s.slot(lag)
                        wait_alone(sp, read["query"], s.count(1, lag), (stacks_ready, 1))
                        for half, tile in enumerate((q_hi, q_lo)):
                            sp.dma_start(q_out[half].rearrange("(m p) n -> p m n", p=128)[:, :, bass.ts(s.item(lag), T)],
                                         tile[:, p]).then_inc(side_stored[p], 16)
                    if not is_self:
                        row(s, 0)
                    if not is_self and s.live(reads["score"][1]):
                        lag = reads["score"][1]
                        p = s.slot(lag)
                        wait(sp, read["score"], s.count(1, lag))
                        sp.dma_start(score_out[bass.ts(s.item(lag), T), :], score[:, p]).then_inc(side_stored[p], 16)

                run(sp, body)
                for p in range(nb):
                    uses = (B - 1 - p) // nb + 1
                    sp.wait_ge(x_stored[p], 16 * uses)
                    sp.wait_ge(side_stored[p], 16 * side_stores * uses)
                for e in range(2 if is_self else 0):
                    sp.wait_ge(ew_stored[e], 16 * (B // 2))

            @block.gpsimd
            def _(pool):
                pool.memset(kst[STACK:STACK + 1], 1.0).then_inc(ident_ready, 1)
                pool.wait_ge(ident_ready, 1)
                pool.memset(val[:], 0.0).then_inc(ident_ready, 1)
                pool.wait_ge(ident_ready, 2)
                for i, constant in enumerate((-0.5, EPS, -1.0)):
                    pool.memset(power[:, i:i + 1], constant).then_inc(ident_ready, 1)
                pool.memset(ident[:], 0.0).then_inc(ident_ready, 1)
                pool.wait_ge(ident_ready, 6)
                pool.affine_select(out=ident[:], in_=ident[:], compare_op=ALU.not_equal, fill=1.0, base=0,
                                   pattern=[[-1, 128]], channel_multiplier=1).then_inc(ident_ready, 1)
                pool.wait_ge(consts_loaded, 16 * consts)

                def body(s):
                    lag = 0
                    if s.live(lag):
                        p = s.slot(lag)
                        wait(pool, x_loaded[p], s.uses(lag) * 16)
                        wait(pool, read["proj"], s.count(1, lag - nb))
                        pool.tensor_tensor(x_bias[:, p], x_in[:, p], b_out[:], ALU.add).then_inc(x_bias_ready, 1)
                    lag = ln_lag
                    if s.live(lag):
                        p = s.slot(lag)
                        wait(pool, mv_ready, s.count(1, lag))
                        pool.tensor_tensor(small[:, p, 0:1], mv[:, p, 1:2], power[:, 1:2], ALU.add).then_inc(small_ready, 1)
                        wait(pool, small_ready, s.count(4, lag, 1))
                        pool.tensor_tensor(small[:, p, 1:2], small[:, p, 0:1], power[:, 0:1], ALU.pow).then_inc(small_ready, 1)
                        wait(pool, small_ready, s.count(4, lag, 2))
                        pool.tensor_tensor(small[:, p, 2:3], mv[:, p, 0:1], small[:, p, 1:2], ALU.mult).then_inc(small_ready, 1)
                        wait(pool, small_ready, s.count(4, lag, 3))
                        pool.tensor_tensor(small[:, p, 3:4], small[:, p, 2:3], power[:, 2:3], ALU.mult).then_inc(small_ready, 1)

                run(pool, body)

            @block.scalar
            def _(act):
                act.wait_ge(consts_loaded, 16 * consts)
                if is_self:
                    nc.scalar.activation(wq_hi[:], wq_f[:], ACT.Copy).then_inc(wq_hi_ready, 1)
                else:
                    act.wait_ge(lam_ready, 2)
                    nc.scalar.activation(lam[:, 2:4], lam[:, 0:2], ACT.Exp).then_inc(lam_ready, 1)

                def ew_uses(s):
                    return s.item() // 2 + 1 if s.m is None else s.m * (nb // 2) + (s.c // 2 + 1)

                def body(s):
                    for e in range(parts):
                        if is_self and s.live():
                            k, cols = s.slot() % 2, slice(e * piece, (e + 1) * piece)
                            if e == 0:
                                wait(act, ew_loaded[k], ew_uses(s) * 16)
                                wait(act, ew_stored[k], (ew_uses(s) - 1) * 16)
                            nc.scalar.activation(ew_half[:, k, 0, cols], ew[:, k, cols], ACT.Copy,
                                                 scale=WSCALE).then_inc(ew_hi_ready, 1)
                        if s.live():
                            n = e % PROBS
                            wait(act, scores_full, s.count(parts, 0, e + 1))
                            wait(act, probs_used, s.count(parts, 0, e + 1 - PROBS))
                            nc.scalar.activation(probs[:, n], bank_score[e % 2][0:rows, 0:4 * T], ACT.Exp,
                                                 scale=sh.scale).then_inc(probs_ready, 1)
                        for h in range(sh.halves):
                            lag = -1 if h == sh.halves - 1 else 0
                            if e == (last_evac if lag else first_evac) and s.live(lag):
                                bank, o = (s.slot(lag) % 2, s.slot(lag) % 2) if is_self else (h, h)
                                wait(act, probs_used, s.count(parts, lag, (h + 1) * parts // sh.halves))
                                wait(act, full[f"out{h}"], s.count(1, lag - (2 if is_self else 1)))
                                nc.scalar.activation(outs[:, o], bank_out[bank][:, 0:4 * T], ACT.Copy).then_inc(out_read[h], 1)
                        if e == norm_part and s.live(ln_lag):
                            lag = ln_lag
                            p = s.slot(lag)
                            wait(act, x_stored[p], (s.uses(lag) - 1) * 16)
                            wait(act, full["turn"], s.count(1, lag - nb))
                            wait(act, small_ready, s.count(4, lag))
                            nc.scalar.activation(y[:, p], r[:, p], ACT.Identity, scale=small[:, p, 1:2],
                                                 bias=small[:, p, 3:4]).then_inc(y_ready, 1)
                        for name, (at, lag) in reads.items():
                            if at != e or not s.live(lag):
                                continue
                            p, bank = s.slot(lag), bank_of(name)
                            if name in ("row0", "row1"):
                                h = int(name[-1])
                                wait(act, full[name], s.count(1, lag))
                                wait(act, row_loaded[h][p], (s.uses(lag) - 1) * 16)
                                nc.scalar.activation(neg_mx[:, p, h], bank[0:16, 0:T], ACT.Copy, scale=-1.0).then_inc(read[name], 1)
                            elif name == "heads":
                                wait(act, full[name], s.count(1, lag))
                                wait(act, full["proj"], s.count(1, lag - nb))
                                nc.scalar.activation(heads_t[:, p], bank[:, 0:KD * T].rearrange("p (k t) -> p k t", k=KD),
                                                     ACT.Copy).then_inc(read[name], 1)
                            elif name == "turn":
                                turned = bank[:, 0:KD * T].rearrange("p (k t) -> p k t", k=KD)
                                wait(act, full[name], s.count(1, lag))
                                if is_self:
                                    wait(act, full["query"], s.count(1, lag - nb))
                                    nc.scalar.activation(y_hi[:, p], turned, ACT.Copy).then_inc(y_hi_ready, 1)
                                else:
                                    wait(act, full["score"], s.count(1, lag - nb))
                                    nc.scalar.activation(y_t[:, p], turned, ACT.Copy).then_inc(read[name], 1)
                            elif name == "query":
                                wait(act, full[name], s.count(1, lag))
                                wait(act, side_stored[p], (s.uses(lag) - 1) * (16 * side_stores))
                                for m in range(KD):
                                    nc.scalar.activation(q_hi[:, p, m], bank[:, m * T:(m + 1) * T], ACT.Identity,
                                                         bias=bq_t[:, m:m + 1]).then_inc(q_hi_ready, 1)
                            elif name == "score":
                                wait(act, full[name], s.count(1, lag))
                                wait(act, side_stored[p], (s.uses(lag) - 1) * (16 * side_stores))
                                nc.scalar.activation(score[:, p], bank[0:T, 0:EXP], ACT.Copy).then_inc(read[name], 1)

                run(act, body)

            @block.vector
            def _(dve):
                nc.vector.memset(qst[:], 0.0).then_inc(stacks_ready, 1)
                if is_self:
                    dve.wait_ge(wq_hi_ready, 1)
                    nc.vector.tensor_tensor(wq_lo[:], wq_f[:], wq_hi[:], ALU.subtract).then_inc(consts_ready, 1)
                else:
                    dve.wait_ge(consts_loaded, 16 * consts)
                    for i in range(2):
                        nc.vector.tensor_tensor(lam_prod[:, i], lam_in[:, 2 * i], lam_in[:, 2 * i + 1], ALU.mult).then_inc(prod_ready, 1)
                    dve.wait_ge(prod_ready, 2)
                    for i in range(2):
                        nc.vector.tensor_reduce(lam[:, i:i + 1], lam_prod[:, i], AX.X, ALU.add).then_inc(lam_ready, 1)
                    dve.wait_ge(lam_ready, 3)
                    nc.vector.tensor_tensor(lam[:, 4:5], lam[:, 2:3], lam[:, 3:4], ALU.subtract).then_inc(lam_ready, 1)
                    dve.wait_ge(lam_ready, 4)
                    nc.vector.tensor_scalar(lam[:, 5:6], lam[:, 4:5], LAMBDA_INIT, LAMBDA_INIT - 1.0,
                                            ALU.add, ALU.mult).then_inc(lam_ready, 1)
                    nc.vector.memset(coef[:], 1.0 - LAMBDA_INIT).then_inc(lam_ready, 1)
                    dve.wait_ge(lam_ready, 6)
                    nc.vector.tensor_scalar(coef[:, :, 1:2], coef[:, :, 1:2], 1.0 / (1.0 - LAMBDA_INIT), lam[:, 5:6],
                                            ALU.mult, ALU.mult).then_inc(consts_ready, 1)
                dve.wait_ge(consts_ready, 1)

                def normalise(s, lag, h, name):
                    p, bank = s.slot(lag), bank_of(name)
                    hn = sh.halves
                    us = slice(16 * h, 16 * h + 16)
                    unit = bank[0:T, :].rearrange("p (u w) -> p u w", w=32)
                    wait(dve, full[name], s.count(1, lag))
                    nc.vector.reciprocal(recip[:, p, us], unit[:, :, DH]).then_inc(recip_ready, 1)
                    wait(dve, recip_ready, order(s, lag, h))
                    if is_self:
                        wait(dve, full["heads"], s.count(1, lag - nb))
                        nc.vector.tensor_tensor(heads[:, p].rearrange("p (u w) -> p u w", w=DH), unit[:, :, 0:DH],
                                                recip[:, p][:, :, None].to_broadcast([T, 16, DH]), ALU.mult).then_inc(read[name], 1)
                        return
                    nc.vector.tensor_tensor(weight[:, p, us], recip[:, p, us], coef[:].rearrange("p a b -> p (a b)"),
                                            ALU.mult).then_inc(weight_ready, 1)
                    wait(dve, weight_ready, order(s, lag, h))
                    if h == 1:
                        wait(dve, heads_ready, s.count(2, lag, 1))
                    nc.vector.tensor_tensor(prod[:, p], unit[:, :, 0:DH], weight[:, p, us][:, :, None].to_broadcast([T, 16, DH]),
                                            ALU.mult).then_inc(read[name], 1)
                    wait(dve, read[name], s.count(1, lag))
                    wait(dve, full["heads"], s.count(1, lag - nb))
                    both = prod[:, p].rearrange("p (h i) w -> p h i w", i=2)
                    nc.vector.tensor_tensor(heads[:, p, 128 * h:128 * h + 128].rearrange("p (h w) -> p h w", w=DH),
                                            both[:, :, 0], both[:, :, 1], ALU.add).then_inc(heads_ready, 1)

                def order(s, lag, h):
                    if is_self:
                        return s.count(1, lag)
                    return s.count(2, lag, 1 if h == 0 else 2)

                def body(s):
                    for e in range(parts):
                        g, c = divmod(e, chunks)
                        if e == aggregate_part and s.live(ln_lag):
                            wait(dve, stats_ready, s.count(1, ln_lag))
                        if s.live(lead):
                            p = s.slot(lead)
                            if is_self:
                                wait(dve, max_full, s.count(groups, lead, g + 1))
                                nc.vector.tensor_reduce(mx[:, p, 4 * g:4 * g + 4],
                                                        max_bank(p, g)[0:T, 0:4 * T].rearrange("p (i t) -> p i t", t=T),
                                                        AX.X, ALU.max).then_inc(max_read, 1)
                            else:
                                for i in ((0, 1), (2,), (3,))[c]:
                                    wait(dve, max_full, s.count(4 * groups, lead, 4 * g + i + 1))
                                    nc.vector.tensor_reduce(mx[:, p, 4 * g + i:4 * g + i + 1], max_bank(p, 4 * g + i)[0:T, 0:S],
                                                            AX.X, ALU.max).then_inc(max_read, 1)
                        if is_self and s.live():
                            k, cols = s.slot() % 2, slice(e * piece, (e + 1) * piece)
                            wait(dve, ew_hi_ready, s.count(parts, 0, e + 1))
                            nc.vector.scalar_tensor_tensor(out=ew_half[:, k, 1, cols], in0=ew[:, k, cols], scalar=WSCALE,
                                                           in1=ew_half[:, k, 0, cols], op0=ALU.mult,
                                                           op1=ALU.subtract).then_inc(ew_ready, 1)
                        if e == aggregate_part and s.live(ln_lag):
                            p = s.slot(ln_lag)
                            nc.vector.bn_aggr(mv[:, p], stats[:, p]).then_inc(mv_ready, 1)
                        for name, (at, lag) in reads.items():
                            if at != e or not s.live(lag):
                                continue
                            p, bank = s.slot(lag), bank_of(name)
                            if name in ("out0", "out1"):
                                normalise(s, lag, int(name[-1]), name)
                            elif name == "proj":
                                wait(dve, full[name], s.count(1, lag))
                                wait(dve, x_bias_ready, s.count(1, lag))
                                wait(dve, y_ready, s.count(1, lag - nb))
                                nc.vector.tensor_tensor(r[:, p], bank[0:T, 0:D], x_bias[:, p], ALU.add).then_inc(read[name], 1)
                                wait(dve, read[name], s.count(1, lag))

                                nc.vector.bn_stats(stats[:, p], r[:, p]).then_inc(stats_ready, 1)
                            elif name == "turn" and is_self:
                                wait(dve, y_hi_ready, s.count(1, lag))
                                wait(dve, full["query"], s.count(1, lag - nb))
                                nc.vector.tensor_tensor(y_lo[:, p], bank[:, 0:KD * T].rearrange("p (k t) -> p k t", k=KD),
                                                        y_hi[:, p], ALU.subtract).then_inc(read[name], 1)
                            elif name == "query":
                                wait(dve, q_hi_ready, s.count(KD, lag))
                                wait(dve, side_stored[p], (s.uses(lag) - 1) * (16 * side_stores))
                                for m in range(KD):
                                    ins = nc.vector.scalar_tensor_tensor(
                                        out=q_lo[:, p, m], in0=bank[:, m * T:(m + 1) * T], scalar=bq_t[:, m:m + 1],
                                        in1=q_hi[:, p, m], op0=ALU.add, op1=ALU.subtract)
                                ins.then_inc(read[name], 1)

                run(dve, body)

            @block.tensor
            def _(pe):
                pe.wait_ge(ident_ready, 7)
                pe.wait_ge(consts_ready, 1)
                pe.wait_ge(stacks_ready, 1)

                def scores(s, e):
                    g, c = divmod(e, chunks)
                    p = s.slot()
                    if e == 0:
                        wait(pe, loaded[p], loaded_value(s, 0))
                    if g % (groups // sh.halves) == 0 and c == 0:
                        wait(pe, row_loaded[g * sh.halves // groups][p], s.uses() * 16)
                    wait(pe, probs_ready, s.count(parts, 0, e - 1))
                    for n, pair in enumerate(pairs_of(g)):
                        last = nc.tensor.matmul(bank_score[e % 2][0:rows, n * pair_w:(n + 1) * pair_w],
                                                kst[:, p, pair, c * rows:(c + 1) * rows], qst[:, p, pair, :],
                                                start=True, stop=True)
                    last.then_inc(scores_full, 1)

                def maxima(s, e):
                    g, c = divmod(e, chunks)
                    p = s.slot(lead)
                    if e == 0:
                        wait(pe, loaded[p], loaded_value(s, lead))
                    if is_self:
                        wait(pe, max_read, s.count(groups, lead, g - 1))
                        for i in range(4):
                            pair, u = 2 * g + i // 2, i % 2
                            last = nc.tensor.matmul(max_bank(p, g)[0:T, i * T:(i + 1) * T],
                                                    qst[0:STACK, p, pair, u * T:(u + 1) * T], kst[0:STACK, p, pair, :],
                                                    start=True, stop=True)
                        last.then_inc(max_full, 1)
                    else:
                        for i in ((0, 1), (2,), (3,))[c]:
                            wait(pe, max_read, s.count(4 * groups, lead, 4 * g + i + 1 - max_banks))
                            nc.tensor.matmul(max_bank(p, 4 * g + i)[0:T, 0:S], qst[0:STACK, p, g, i * T:(i + 1) * T],
                                             kst[0:STACK, p, g, :], start=True, stop=True).then_inc(max_full, 1)

                def weigh(s, lag, e):
                    g, c = divmod(e, chunks)
                    p = s.slot(lag)
                    per = groups // sh.halves
                    h = g // per
                    bank = bank_out[p % 2 if is_self else h]
                    if g % per == 0 and c == 0:
                        wait(pe, out_read[h], s.count(1, lag - (2 if is_self else 1)))
                    wait(pe, probs_ready, s.count(parts, lag, e + 1))
                    for i in range(4):
                        col = c * VROW + head_of(g, i) * VW
                        last = nc.tensor.matmul(bank[32 * i:32 * i + 32, (g % per) * T:(g % per + 1) * T],
                                                val[:, p, col:col + 32], probs[:, e % PROBS, i * T:(i + 1) * T],
                                                start=c == 0, stop=c == chunks - 1)
                    last.then_inc(probs_used, 1)

                def step(s, name):
                    lag = steps[name][1]
                    p, bank = s.slot(lag), bank_of(name)
                    n = names.index(name)
                    for back in range(n - step_banks, n - 2 * len(names), -step_banks):
                        before, turn_back = names[back % len(names)], back // len(names)
                        if s.live(steps[before][1] + turn_back):
                            wait(pe, read[before], s.count(1, steps[before][1] + turn_back))
                            break
                    if name in ("row0", "row1"):
                        h = int(name[-1])
                        per = groups // sh.halves if is_self else 4 * groups // sh.halves
                        wait(pe, max_read, s.count(per * sh.halves, lag, per * (h + 1)))
                        last = nc.tensor.transpose(bank[0:16, 0:T], mx[:, p, 16 * h:16 * h + 16], ident[0:T, 0:T])
                    elif name in ("out0", "out1"):
                        h = int(name[-1])
                        wait(pe, out_read[h], s.count(1, lag))
                        o = p % 2 if is_self else h
                        for g in range(4):
                            last = nc.tensor.transpose(bank[0:T, 128 * g:128 * g + 128], outs[:, o, g * T:(g + 1) * T], ident[:])
                    elif name == "heads":
                        if is_self:
                            wait(pe, read["out0"], s.count(1, lag))
                        else:
                            wait(pe, heads_ready, s.count(2, lag))
                        for k in range(KD):
                            last = nc.tensor.transpose(bank[:, k * T:(k + 1) * T], heads[:, p, 128 * k:128 * k + 128], ident[0:T, 0:T])
                    elif name == "proj":
                        wait(pe, read["heads"], s.count(1, lag))
                        for k in range(KD):
                            last = nc.tensor.matmul(bank[0:T, 0:D], heads_t[:, p, k], w_out[:, k, :], start=k == 0, stop=k == KD - 1)
                    elif name == "turn":
                        wait(pe, y_ready, s.count(1, lag))
                        for k in range(KD):
                            last = nc.tensor.transpose(bank[:, k * T:(k + 1) * T], y[:, p, 128 * k:128 * k + 128], ident[0:T, 0:T])
                    elif name == "query":
                        wait(pe, read["turn"], s.count(1, lag))
                        terms = [(k, wt, yt) for k in range(KD) for wt, yt in ((wq_hi, y_hi), (wq_lo, y_hi), (wq_hi, y_lo))]
                        for m in range(KD):
                            for n, (k, wt, yt) in enumerate(terms):
                                last = nc.tensor.matmul(bank[:, m * T:(m + 1) * T], wt[:, k, 128 * m:128 * m + 128],
                                                        yt[:, p, k], start=n == 0, stop=n == len(terms) - 1)
                    elif name == "score":
                        wait(pe, read["turn"], s.count(1, lag))
                        for k in range(KD):
                            last = nc.tensor.matmul(bank[0:T, 0:EXP], y_t[:, p, k], gate_w[:, k, :], start=k == 0, stop=k == KD - 1)
                    last.then_inc(full[name], 1)

                def body(s):
                    for e in range(parts):
                        if s.live():
                            scores(s, e)
                        if s.live(lead):
                            maxima(s, e)
                        lag, part = (0, e - sh.lag) if e >= sh.lag else (-1, parts + e - sh.lag)
                        if s.live(lag):
                            weigh(s, lag, part)
                        for name, (at, lag) in steps.items():
                            if at == e and s.live(lag):
                                step(s, name)

                run(pe, body)


ROW = D + 4
CAP = NT + 256
BLOCK = 256
BT = BLOCK // 128
BLOCKS = (2 * NT + EXP * (BLOCK - 1)) // BLOCK
FC = FF // 128
DUMMY = EXP * CAP


def route(nc, scores_in, x2, routed, table_i, table_f):
    BIG = 3.0e38
    JITTER = 0.02
    with ExitStack() as ctx:
        ph = Phase(nc, ctx, "route")
        shape = [T, B, EXP]
        rows = ph.sb("rows", [T, B, ROW], F32)
        names = ("s", "neg", "absv", "d1", "eq1", "pick1", "oh1", "f1", "keep1", "ex1", "s2", "d2", "eq2", "pick2",
                 "oh2", "f2", "keep2", "ex2", "place", "tmp1", "tmp2", "tmp3")
        t = {n: ph.sb(n, shape, F32) for n in names}
        col = {n: ph.sb(n, [T, B], F32) for n in ("m1", "top1", "m2", "top2", "den1", "den2", "slot1", "slot2")}
        both = ph.sb("both", shape, F16)
        slot_i = ph.sb("slot_i", [T, 2, B], I32)
        prio = ph.sb("prio", [T, EXP], F32)
        expert = ph.sb("expert", [T, EXP], F32)
        region = ph.sb("region", [T, EXP], F32)
        token = ph.sb("token", [T, B], F32)
        before = ph.sb("before", [T, T], F16)
        ones = ph.sb("ones", [T, 128], F16)
        onesf = ph.sb("onesf", [128, B], F32)
        total = ph.sb("total", [128, B, EXP], F32)
        running = ph.sb("running", [128, B, EXP], F32)
        steps_i = ph.sb("steps_i", [128, NT // BLOCK], F32)
        block_no = ph.sb("block_no", [128, BLOCKS], F32)
        over = ph.sb("over", [128, EXP, NT // BLOCK], F32)
        nblk = ph.sb("nblk", [128, EXP], F32)
        cum = ph.sb("cum", [128, EXP], F32)
        done = ph.sb("done", [128, BLOCKS, EXP], F32)
        done_n = ph.sb("done_n", [128, BLOCKS, EXP], F32)
        tb = {n: ph.sb(n, [128, BLOCKS], F32) for n in ("first", "used", "off", "off2", "row", "wexp")}
        pad = ph.sb("pad", [128, BT, ROW], F32)
        pad_i = ph.sb("pad_i", [128, EXP], F32)
        pad_row = ph.sb("pad_row", [128, EXP], I32)
        regions = ph.sb("regions", [128, EXP], F32)
        bank_rank, bank_total = ph.ps("bank_rank", [128, 512]), ph.ps("bank_total", [128, 512])
        loaded, rows_loaded, consts_ready, ops, exp_ready, both_ready, counted, placed, scattered, pad_ready, padded = (
            ph.sem(n) for n in ("loaded", "rows_loaded", "consts_ready", "ops", "exp_ready", "both_ready", "counted",
                                "placed", "scattered", "pad_ready", "padded"))
        padding_ready = ph.sem("padding_ready")
        with nc.Block() as block:

            @block.sync
            def _(sp):
                sp.dma_start(t["s"][:], scores_in.rearrange("(b t) e -> t b e", t=T)).then_inc(loaded, 16)
                sp.dma_start(rows[:, :, 0:D], x2.rearrange("(b t) n -> t b n", t=T)[:, :, 0:D]).then_inc(rows_loaded, 16)
                sp.wait_ge(pad_ready, 1)
                sp.wait_ge(padding_ready, 4)
                for e in range(EXP):
                    at = sp.value_load(pad_row[0:1, e:e + 1], min_val=0, max_val=DUMMY - BLOCK)
                    sp.dma_start(routed[bass.ds(at, BLOCK), :].rearrange("(p j) n -> p j n", j=BT), pad[:]).then_inc(padded, 16)
                sp.dma_start(routed[DUMMY:DUMMY + BLOCK, :].rearrange("(p j) n -> p j n", j=BT), pad[:]).then_inc(padded, 16)
                sp.wait_ge(padded, 16 * (EXP + 1))

            @block.gpsimd
            def _(pool):
                small = dict(allow_small_or_imprecise_dtypes=True)
                pool.iota(prio[:], pattern=[[-1, EXP]], base=EXP, channel_multiplier=0, **small).then_inc(consts_ready, 1)
                pool.iota(expert[:], pattern=[[1, EXP]], base=0, channel_multiplier=0, **small).then_inc(consts_ready, 1)
                pool.iota(region[:], pattern=[[CAP, EXP]], base=0, channel_multiplier=0, **small).then_inc(consts_ready, 1)
                pool.iota(regions[:], pattern=[[CAP, EXP]], base=0, channel_multiplier=0, **small).then_inc(consts_ready, 1)
                pool.iota(token[:], pattern=[[T, B]], base=0, channel_multiplier=1, **small).then_inc(consts_ready, 1)
                pool.iota(steps_i[:], pattern=[[BLOCK, NT // BLOCK]], base=0, channel_multiplier=0, **small).then_inc(consts_ready, 1)
                pool.iota(block_no[:], pattern=[[1, BLOCKS]], base=0, channel_multiplier=0, **small).then_inc(consts_ready, 1)
                pool.memset(ones[:], 1.0).then_inc(consts_ready, 1)
                pool.memset(onesf[:], 1.0).then_inc(consts_ready, 1)
                pool.wait_ge(consts_ready, 9)
                pool.affine_select(out=before[:], in_=ones[:, 0:T], compare_op=ALU.is_gt, fill=0.0, base=0,
                                   pattern=[[1, T]], channel_multiplier=-1).then_inc(consts_ready, 1)
                pool.memset(pad[:], 0.0).then_inc(padding_ready, 1)
                pool.wait_ge(padding_ready, 1)
                pool.iota(pad[:, :, D:D + 1], pattern=[[1, BT], [0, 1]], base=2 * NT, channel_multiplier=BT, **small).then_inc(padding_ready, 1)
                pool.wait_ge(padding_ready, 2)
                pool.memset(pad[:, :, D + 1:D + 2], -1.0).then_inc(padding_ready, 1)
                pool.wait_ge(padding_ready, 3)
                pool.memset(pad[:, :, D + 2:ROW], 0.0).then_inc(padding_ready, 1)
                pool.wait_ge(placed, 6)
                for b in range(B):
                    for c in range(2):
                        pool.indirect_dma_start(routed[:, :], bass.IndirectOffsetOnAxis(ap=slot_i[:, c, b:b + 1], axis=0),
                                                rows[:, b, :], None).then_inc(scattered, 16)
                pool.wait_ge(scattered, 32 * B)

            @block.scalar
            def _(act):
                for n, (d, ex) in enumerate((("d1", "ex1"), ("d2", "ex2"))):
                    act.wait_ge(exp_ready, 2 * n + 1)
                    nc.scalar.activation(t[ex][:], t[d][:], ACT.Exp, scale=-1.0).then_inc(exp_ready, 1)

            @block.tensor
            def _(pe):
                pe.wait_ge(both_ready, 1)
                pe.wait_ge(consts_ready, 10)
                flat = both[:].rearrange("p b e -> p (b e)")
                nc.tensor.matmul(bank_rank[0:T, 0:B * EXP], before[:], flat, start=True, stop=True)
                nc.tensor.matmul(bank_total[:, 0:B * EXP], ones[:], flat, start=True, stop=True).then_inc(counted, 1)

            @block.vector
            def _(dve):
                n_ops = [0]

                def then(ins):
                    n_ops[0] += 1
                    ins.then_inc(ops, 1)
                    dve.wait_ge(ops, n_ops[0])

                def over_e(x):
                    return x[:, :, None].to_broadcast(shape)

                def over_b(x):
                    return x[:, None, :].to_broadcast(shape)

                tt, v = nc.vector.tensor_tensor, nc.vector
                dve.wait_ge(loaded, 16)
                dve.wait_ge(consts_ready, 10)
                s = t["s"][:]
                then(v.tensor_reduce(col["m1"][:], s, AX.X, ALU.max))
                then(tt(t["d1"][:], over_e(col["m1"][:]), s, ALU.subtract))
                tt(t["eq1"][:], over_e(col["m1"][:]), s, ALU.is_equal).then_inc(exp_ready, 1)
                then(v.scalar_tensor_tensor(out=t["absv"][:], in0=s, scalar=-1.0, in1=s, op0=ALU.mult, op1=ALU.max))
                then(tt(t["pick1"][:], t["eq1"][:], over_b(prio[:]), ALU.mult))
                then(v.tensor_reduce(col["top1"][:], t["pick1"][:], AX.X, ALU.max))
                then(tt(t["oh1"][:], t["pick1"][:], over_e(col["top1"][:]), ALU.is_equal))
                then(tt(t["f1"][:], t["absv"][:], over_e(col["m1"][:]), ALU.max))
                then(v.scalar_tensor_tensor(out=t["keep1"][:], in0=t["f1"][:], scalar=JITTER, in1=t["d1"][:],
                                            op0=ALU.mult, op1=ALU.is_ge))
                then(v.scalar_tensor_tensor(out=t["s2"][:], in0=t["oh1"][:], scalar=-BIG, in1=s, op0=ALU.mult, op1=ALU.add))
                then(v.tensor_reduce(col["m2"][:], t["s2"][:], AX.X, ALU.max))
                then(tt(t["d2"][:], over_e(col["m2"][:]), t["s2"][:], ALU.subtract))
                dve.wait_ge(exp_ready, 2)
                tt(t["eq2"][:], over_e(col["m2"][:]), t["s2"][:], ALU.is_equal).then_inc(exp_ready, 1)
                then(tt(t["f2"][:], t["absv"][:], over_e(col["m2"][:]), ALU.max))
                then(tt(t["pick2"][:], t["eq2"][:], over_b(prio[:]), ALU.mult))
                then(v.tensor_reduce(col["top2"][:], t["pick2"][:], AX.X, ALU.max))
                then(tt(t["oh2"][:], t["pick2"][:], over_e(col["top2"][:]), ALU.is_equal))
                tt(both[:], t["oh1"][:], t["oh2"][:], ALU.add).then_inc(both_ready, 1)
                then(v.scalar_tensor_tensor(out=t["keep2"][:], in0=t["f2"][:], scalar=JITTER, in1=t["d2"][:],
                                            op0=ALU.mult, op1=ALU.is_ge))
                dve.wait_ge(exp_ready, 4)
                then(tt(t["tmp1"][:], t["ex1"][:], t["keep1"][:], ALU.mult))
                then(tt(t["tmp2"][:], t["ex2"][:], t["keep2"][:], ALU.mult))
                then(v.tensor_reduce(col["den1"][:], t["tmp1"][:], AX.X, ALU.add))
                then(v.tensor_reduce(col["den2"][:], t["tmp2"][:], AX.X, ALU.add))
                dve.wait_ge(rows_loaded, 16)
                v.reciprocal(rows[:, :, D + 2], col["den1"][:]).then_inc(placed, 1)
                v.reciprocal(rows[:, :, D + 3], col["den2"][:]).then_inc(placed, 1)
                v.tensor_copy(rows[:, :, D], token[:]).then_inc(placed, 1)
                then(tt(t["tmp3"][:], t["oh1"][:], over_b(expert[:]), ALU.mult))
                v.tensor_reduce(rows[:, :, D + 1], t["tmp3"][:], AX.X, ALU.add).then_inc(placed, 1)
                dve.wait_ge(counted, 1)
                then(v.tensor_copy(total[:].rearrange("p b e -> p (b e)"), bank_total[:, 0:B * EXP]))
                for e in range(EXP):
                    last = v.tensor_tensor_scan(running[:, :, e], onesf[:], total[:, :, e], 0.0, ALU.mult, ALU.add)
                then(last)
                then(tt(t["place"][:].rearrange("p b e -> p (b e)"), bank_rank[0:T, 0:B * EXP],
                        running[0:T].rearrange("p b e -> p (b e)"), ALU.add))
                then(tt(t["tmp1"][:], t["place"][:], total[0:T], ALU.subtract))
                then(tt(t["tmp2"][:], t["tmp1"][:], over_b(region[:]), ALU.add))
                then(tt(t["tmp3"][:], t["tmp2"][:], t["oh1"][:], ALU.mult))
                then(tt(t["tmp1"][:], t["tmp2"][:], t["oh2"][:], ALU.mult))
                then(v.tensor_reduce(col["slot1"][:], t["tmp3"][:], AX.X, ALU.add))
                then(v.tensor_reduce(col["slot2"][:], t["tmp1"][:], AX.X, ALU.add))
                v.tensor_copy(slot_i[:, 0], col["slot1"][:]).then_inc(placed, 1)
                v.tensor_copy(slot_i[:, 1], col["slot2"][:]).then_inc(placed, 1)
                rows_of = running[:, B - 1, :]
                then(tt(pad_i[:], rows_of, regions[:], ALU.add))
                v.tensor_copy(pad_row[:], pad_i[:]).then_inc(pad_ready, 1)
                n_steps = NT // BLOCK
                then(tt(over[:], rows_of[:, :, None].to_broadcast([128, EXP, n_steps]),
                        steps_i[:, None, :].to_broadcast([128, EXP, n_steps]), ALU.is_gt))
                then(v.tensor_reduce(nblk[:], over[:], AX.X, ALU.add))
                then(v.tensor_tensor_scan(cum[:], onesf[:, 0:EXP], nblk[:], 0.0, ALU.mult, ALU.add))
                then(tt(done[:], cum[:, None, :].to_broadcast([128, BLOCKS, EXP]),
                        block_no[:, :, None].to_broadcast([128, BLOCKS, EXP]), ALU.is_le))
                then(tt(done_n[:], done[:], nblk[:, None, :].to_broadcast([128, BLOCKS, EXP]), ALU.mult))
                then(v.tensor_reduce(table_f[:, 0], done[:], AX.X, ALU.add))
                then(v.tensor_reduce(tb["first"][:], done_n[:], AX.X, ALU.add))
                then(v.tensor_scalar(tb["used"][:], table_f[:, 0], float(EXP), float(BLOCK), ALU.is_lt, ALU.mult))
                then(tt(tb["off"][:], block_no[:], tb["first"][:], ALU.subtract))
                then(tt(tb["off2"][:], tb["off"][:], tb["used"][:], ALU.mult))
                then(v.scalar_tensor_tensor(out=tb["row"][:], in0=table_f[:, 0], scalar=float(CAP), in1=tb["off2"][:],
                                            op0=ALU.mult, op1=ALU.add))
                then(v.tensor_scalar(tb["wexp"][:], table_f[:, 0], float(EXP - 1), float(CUTS), ALU.min, ALU.mult))
                v.tensor_scalar(table_f[:, 1], block_no[:], float(BLOCK), None, ALU.mult)
                then(v.tensor_copy(table_i[:, 0], tb["row"][:]))
                then(v.tensor_copy(table_i[:, 1], tb["wexp"][:]))


def experts(nc, routed, weights, table_i, table_f, y_out):
    with ExitStack() as ctx:
        ph = Phase(nc, ctx, "experts")
        w = ph.sb("w", [128, 2, CUTS, 2, CUT], F16)
        rows = ph.sb("rows", [128, 2, BT, ROW], F32)
        x_hi = ph.sb("x_hi", [128, 2, KD, BLOCK], F16)
        x_lo = ph.sb("x_lo", [128, 2, KD, BLOCK], F16)
        gated = ph.sb("gated", [128, 2, BLOCK], F32)
        hid = ph.sb("hid", [128, 2, BLOCK], F32)
        h_hi = ph.sb("h_hi", [128, 2, FC, BLOCK], F16)
        h_lo = ph.sb("h_lo", [128, 2, FC, BLOCK], F16)
        first = ph.sb("first", [128, 2, BT], F32)
        other = ph.sb("other", [128, 2, BT], F32)
        part1 = ph.sb("part1", [128, 2, BT], F32)
        part2 = ph.sb("part2", [128, 2, BT], F32)
        share = ph.sb("share", [128, 2, BT], F32)
        token = ph.sb("token", [128, 2, BT], F32)
        spare = ph.sb("spare", [128, 2, BT], F32)
        dest_i = ph.sb("dest_i", [128, 2, BT], I32)
        y = ph.sb("y", [128, 2, BT, D], F32)
        ident = ph.sb("ident", [128, 128], F32)
        bank_x = ph.ps("bank_x", [128, 512])
        bank_h = [ph.ps(f"bank_h{i}", [128, 512]) for i in range(4)]
        bank_y = [ph.ps(f"bank_y{i}", [128, 512]) for i in range(BT)]
        ident_ready = ph.sem("ident_ready")
        w_loaded, rows_loaded, y_stored = ph.sems("w_loaded", 2), ph.sems("rows_loaded", 2), ph.sems("y_stored", 2)
        x_turned, x_hi_ready, x_ready, h_full, gated_ready, hid_ready, h_hi_ready, h_ready, y_full, y_ready = (
            ph.sem(n) for n in ("x_turned", "x_hi_ready", "x_ready", "h_full", "gated_ready", "hid_ready",
                                "h_hi_ready", "h_ready", "y_full", "y_ready"))
        meta, meta2, meta_done = (ph.sem(n) for n in ("meta", "meta2", "meta_done"))

        def cols(p, half, col, n):
            return w[:, p, col // CUT, half, col % CUT:col % CUT + n]

        w13 = lambda p, half, mat, k, f: cols(p, half, (mat * KD + k) * FF + f * 128, 128)
        w2 = lambda p, half, f: cols(p, half, 2 * KD * FF + f * D, D)

        with nc.Block() as block:

            @block.sync
            def _(sp):
                def body(s):
                    if not s.live(1):
                        return
                    p, j = s.slot(1), s.item(1)
                    row = sp.value_load(table_i[0:1, 0, bass.ds(j, 1)], min_val=0, max_val=DUMMY)
                    expert = sp.value_load(table_i[0:1, 1, bass.ds(j, 1)], min_val=0, max_val=CUTS * (EXP - 1))
                    wait(sp, x_turned, s.count(1, -1))
                    wait_alone(sp, meta_done, s.count(1, -1), (ident_ready, 2))
                    sp.dma_start(rows[:, p], routed[bass.ds(row, BLOCK), :].rearrange("(i p) n -> p i n", p=128)).then_inc(rows_loaded[p], 16)
                    wait_alone(sp, y_full, s.count(BT, -1), (ident_ready, 2))
                    sp.dma_start(w[:, p].rearrange("p q h n -> p q (h n)"), weights[bass.ds(expert, CUTS)].rearrange("q p h n -> p q (h n)")).then_inc(w_loaded[p], 16)

                pipeline(sp, body, BLOCKS, 2, 3, 1, 0)

            @block.gpsimd
            def _(pool):
                pool.memset(ident[:], 0.0).then_inc(ident_ready, 1)
                pool.wait_ge(ident_ready, 1)
                pool.affine_select(out=ident[:], in_=ident[:], compare_op=ALU.not_equal, fill=1.0, base=0,
                                   pattern=[[-1, 128]], channel_multiplier=1).then_inc(ident_ready, 1)
                scatters = pool.alloc_register("scatters")
                pool.reg_mov(scatters, 0)

                def body(s):
                    if not s.live():
                        return
                    p = s.slot()
                    wait(pool, meta_done, s.count(1))
                    for i in range(BT):
                        pool.reg_add(scatters, scatters, 1)
                        pool.wait_ge(ident_ready, 2)
                        pool.wait_ge(y_ready, scatters)
                        pool.indirect_dma_start(y_out[:, :], bass.IndirectOffsetOnAxis(ap=dest_i[:, p, i:i + 1], axis=0),
                                                y[:, p, i], None).then_inc(y_stored[p], 16)

                pipeline(pool, body, BLOCKS, 2, 3, 1, 0)
                for p in range(2):
                    pool.wait_ge(y_stored[p], 16 * BT * ((BLOCKS - p + 1) // 2))

            @block.scalar
            def _(act):
                def x_high(s):
                    p = s.slot(1)
                    wait(act, x_turned, s.count(1, 1))
                    wait(act, h_full, s.count(FC, -1))
                    nc.scalar.activation(x_hi[:, p], bank_x[:].rearrange("p (k t) -> p k t", k=KD), ACT.Copy).then_inc(x_hi_ready, 1)

                def h_high(s, f):
                    p = s.slot()
                    wait(act, hid_ready, s.count(FC, 0, f + 1))
                    wait(act, y_full, s.count(BT, -2))
                    nc.scalar.activation(h_hi[:, p, f], hid[:, f % 2], ACT.Copy).then_inc(h_hi_ready, 1)

                def body(s):
                    if s.live():
                        for f in range(FC):
                            wait(act, h_full, s.count(FC, 0, f + 1))
                            wait(act, hid_ready, s.count(FC, 0, f - 1))
                            nc.scalar.activation(gated[:, f % 2], bank_h[f % 4][:, 0:BLOCK], ACT.Silu,
                                                 scale=1.0 / WSCALE).then_inc(gated_ready, 1)
                            if f:
                                h_high(s, f - 1)
                            if f == 4 and s.live(1):
                                x_high(s)
                        h_high(s, FC - 1)
                        p = s.slot()
                        wait(act, meta_done, s.count(1))
                        for i in range(BT):
                            wait(act, y_full, s.count(BT, 0, i + 1))
                            wait(act, y_stored[p], (s.uses() - 1) * (16 * BT))
                            nc.scalar.activation(y[:, p, i], bank_y[i][:, 0:D], ACT.Copy, scale=share[:, p, i:i + 1]).then_inc(y_ready, 1)
                    elif s.live(1):
                        x_high(s)

                pipeline(act, body, BLOCKS, 2, 3, 1, 0)

            @block.vector
            def _(dve):
                def x_low(s):
                    p = s.slot(1)
                    wait(dve, x_hi_ready, s.count(1, 1))
                    wait(dve, h_full, s.count(FC, -1))
                    nc.vector.tensor_tensor(x_lo[:, p], bank_x[:].rearrange("p (k t) -> p k t", k=KD), x_hi[:, p],
                                            ALU.subtract).then_inc(x_ready, 1)

                def h_low(s, f):
                    p = s.slot()
                    wait(dve, h_hi_ready, s.count(FC, 0, f + 1))
                    nc.vector.tensor_tensor(h_lo[:, p, f], hid[:, f % 2], h_hi[:, p, f], ALU.subtract).then_inc(h_ready, 1)

                def destinations(s):
                    p, j = s.slot(), s.item()
                    col = lambda c: rows[:, p, :, D + c]
                    wait(dve, rows_loaded[p], s.uses() * 16)
                    wait(dve, y_stored[p], (s.uses() - 1) * (16 * BT))
                    nc.vector.tensor_tensor(first[:, p], col(1), table_f[:, 0, bass.ds(j, 1)].to_broadcast([128, BT]), ALU.is_equal).then_inc(meta, 1)
                    wait(dve, meta, s.count(6, 0, 1))
                    nc.vector.tensor_scalar(other[:, p], first[:, p], -1.0, 1.0, ALU.mult, ALU.add).then_inc(meta, 1)
                    nc.vector.tensor_tensor(part1[:, p], first[:, p], col(2), ALU.mult).then_inc(meta, 1)
                    wait(dve, meta, s.count(6, 0, 3))
                    nc.vector.tensor_tensor(part2[:, p], other[:, p], col(3), ALU.mult).then_inc(meta, 1)
                    nc.vector.scalar_tensor_tensor(out=token[:, p], in0=other[:, p], scalar=float(NT), in1=col(0),
                                                   op0=ALU.mult, op1=ALU.add).then_inc(meta, 1)
                    nc.vector.scalar_tensor_tensor(out=spare[:, p], in0=col(1), scalar=0.0,
                                                   in1=table_f[:, 1, bass.ds(j, 1)].to_broadcast([128, BT]),
                                                   op0=ALU.is_lt, op1=ALU.mult).then_inc(meta, 1)
                    wait(dve, meta, s.count(6))
                    nc.vector.tensor_tensor(dest_i[:, p], token[:, p], spare[:, p], ALU.add)
                    nc.vector.tensor_tensor(part1[:, p], part1[:, p], part2[:, p], ALU.add).then_inc(meta2, 1)
                    wait(dve, meta2, s.count(1))
                    nc.vector.tensor_scalar(share[:, p], part1[:, p], 1.0 / (WSCALE * WSCALE), None, ALU.mult).then_inc(meta_done, 1)

                def body(s):
                    if s.live():
                        for f in range(FC):
                            wait(dve, gated_ready, s.count(FC, 0, f + 1))
                            wait(dve, h_ready, s.count(FC, 0, f - 1))
                            nc.vector.tensor_tensor(hid[:, f % 2], bank_h[f % 4][:, BLOCK:2 * BLOCK], gated[:, f % 2],
                                                    ALU.mult).then_inc(hid_ready, 1)
                            if f:
                                h_low(s, f - 1)
                            if f == 2:
                                destinations(s)
                            if f == 4 and s.live(1):
                                x_low(s)
                        h_low(s, FC - 1)
                    elif s.live(1):
                        x_low(s)

                pipeline(dve, body, BLOCKS, 2, 3, 1, 0)

            @block.tensor
            def _(pe):
                pe.wait_ge(ident_ready, 2)

                def turn(s):
                    p = s.slot(1)
                    wait(pe, rows_loaded[p], s.uses(1) * 16)
                    wait(pe, x_ready, s.count(1))
                    for k in range(KD):
                        for i in range(BT):
                            last = nc.tensor.transpose(bank_x[:, k * BLOCK + i * 128:k * BLOCK + i * 128 + 128],
                                                       rows[:, p, i, k * 128:(k + 1) * 128], ident[:])
                    last.then_inc(x_turned, 1)

                def body(s):
                    if not s.live():
                        if s.live(1):
                            turn(s)
                        return
                    p = s.slot()
                    wait(pe, x_ready, s.count(1))
                    wait(pe, w_loaded[p], s.uses() * 16)
                    for f in range(FC):
                        wait(pe, hid_ready, s.count(FC, 0, f - 3))
                        for mat in range(2):
                            terms = [(k, wh, xt) for k in range(KD) for wh, xt in ((0, x_hi), (1, x_hi), (0, x_lo))]
                            for n, (k, wh, xt) in enumerate(terms):
                                last = nc.tensor.matmul(bank_h[f % 4][:, mat * BLOCK:(mat + 1) * BLOCK], w13(p, wh, mat, k, f),
                                                        xt[:, p, k], start=n == 0, stop=n == len(terms) - 1)
                        last.then_inc(h_full, 1)
                        if f == 3 and s.live(1):
                            turn(s)
                    for f in range(FC):
                        wait(pe, h_ready, s.count(FC, 0, f + 1))
                        for i in range(BT):
                            if f == 0:
                                wait(pe, y_ready, s.count(BT, -1, i + 1))
                            for n, (ht, wh) in enumerate(((h_hi, 0), (h_hi, 1), (h_lo, 0))):
                                end = f == FC - 1 and n == TERMS - 1
                                last = nc.tensor.matmul(bank_y[i][:, 0:D], ht[:, p, f, i * 128:(i + 1) * 128], w2(p, wh, f),
                                                        start=f == 0 and n == 0, stop=end)
                                if end:
                                    last.then_inc(y_full, 1)

                pipeline(pe, body, BLOCKS, 2, 3, 1, 0)


def finish(nc, x2, y_in, out):
    per = NT // 128
    chunks = 4
    n = per // chunks
    with ExitStack() as ctx:
        ph = Phase(nc, ctx, "finish")
        x = ph.sb("x", [128, chunks, n, D], F32)
        y1 = ph.sb("y1", [128, chunks, n, D], F32)
        y2 = ph.sb("y2", [128, chunks, n, D], F32)
        r = ph.sb("r", [128, chunks, n, D], F32)
        stats = ph.sb("stats", [128, chunks, n, 6], F32)
        mv = ph.sb("mv", [128, chunks, n, 2], F32)
        var = ph.sb("var", [128, chunks, n], F32)
        rstd = ph.sb("rstd", [128, chunks, n], F32)
        shift = ph.sb("shift", [128, chunks, n], F32)
        consts = ph.sb("consts", [128, 3, n], F32)
        loaded = ph.sems("loaded", chunks)
        stored, consts_ready, half_sum, sum_ready, stats_ready, mv_ready, small, out_ready = (
            ph.sem(s) for s in ("stored", "consts_ready", "half_sum", "sum_ready", "stats_ready", "mv_ready",
                                "small", "out_ready"))
        rows = lambda a: a.rearrange("(p c i) n -> c p i n", c=chunks, i=n)
        with nc.Block() as block:

            @block.sync
            def _(sp):
                for c in range(chunks):
                    sp.dma_start(y1[:, c], rows(y_in[0:NT, :])[c]).then_inc(loaded[c], 16)
                    sp.dma_start(y2[:, c], rows(y_in[NT:2 * NT, :])[c]).then_inc(loaded[c], 16)
                    sp.dma_start(x[:, c], rows(x2)[c, :, :, 0:D]).then_inc(loaded[c], 16)
                for c in range(chunks):
                    sp.wait_ge(out_ready, n * (c + 1))
                    sp.dma_start(rows(out)[c], x[:, c]).then_inc(stored, 16)
                sp.wait_ge(stored, 16 * chunks)

            @block.gpsimd
            def _(pool):
                for i, v in enumerate((EPS, -0.5, -1.0)):
                    pool.memset(consts[:, i], v).then_inc(consts_ready, 1)
                pool.wait_ge(consts_ready, 3)

                def statistics(c):
                    pool.wait_ge(mv_ready, n * (c + 1))
                    pool.tensor_tensor(var[:, c], mv[:, c, :, 1], consts[:, 0], ALU.add).then_inc(small, 1)
                    pool.wait_ge(small, 4 * c + 1)
                    pool.tensor_tensor(rstd[:, c], var[:, c], consts[:, 1], ALU.pow).then_inc(small, 1)
                    pool.wait_ge(small, 4 * c + 2)
                    pool.tensor_tensor(var[:, c], mv[:, c, :, 0], rstd[:, c], ALU.mult).then_inc(small, 1)
                    pool.wait_ge(small, 4 * c + 3)
                    pool.tensor_tensor(shift[:, c], var[:, c], consts[:, 2], ALU.mult).then_inc(small, 1)

                for c in range(chunks):
                    pool.wait_ge(loaded[c], 48)
                    pool.tensor_tensor(y1[:, c], y1[:, c], y2[:, c], ALU.add).then_inc(half_sum, 1)
                    if c:
                        statistics(c - 1)
                statistics(chunks - 1)

            @block.vector
            def _(dve):
                for c in range(chunks):
                    dve.wait_ge(half_sum, c + 1)
                    nc.vector.tensor_tensor(r[:, c], x[:, c], y1[:, c], ALU.add).then_inc(sum_ready, 1)
                    dve.wait_ge(sum_ready, c + 1)
                    for i in range(n):
                        last = nc.vector.bn_stats(stats[:, c, i], r[:, c, i])
                    last.then_inc(stats_ready, 1)
                    dve.wait_ge(stats_ready, c + 1)
                    for i in range(n):
                        nc.vector.bn_aggr(mv[:, c, i], stats[:, c, i]).then_inc(mv_ready, 1)

            @block.scalar
            def _(act):
                for c in range(chunks):
                    act.wait_ge(small, 4 * (c + 1))
                    for i in range(n):
                        nc.scalar.activation(x[:, c, i], r[:, c, i], ACT.Identity, scale=rstd[:, c, i:i + 1],
                                             bias=shift[:, c, i:i + 1]).then_inc(out_ready, 1)


def decoder(nc, a):
    dram = lambda name, shape, dt: nc.dram_tensor(name, shape, dt)
    with ExitStack() as ctx:
        self_q = dram("self_q", [3 * D, NT], F16)
        self_k = dram("self_k", [3 * D, NT], F16)
        self_v = dram("self_v", [NT, VROW], F32)
        cross_q = dram("cross_q", [2, D, NT], F16)
        cross_k = dram("cross_k", [2, D, B * S], F16)
        cross_v = dram("cross_v", [B * S, VROW], F32)
        x1 = dram("x1", [NT, D], F32)
        x2 = dram("x2", [NT, ROW], F32)
        scores = dram("scores", [NT, EXP], F32)
        w_halves = dram("w_halves", [B, 128, 2, CUT], F16)
        routed = dram("routed", [DUMMY + BLOCK, ROW], F32)
        y = dram("y", [3 * NT + BLOCKS * BLOCK, D], F32)
        table_i = ctx.enter_context(nc.sbuf_tensor("table_i", [128, 2, BLOCKS], I32))
        table_f = ctx.enter_context(nc.sbuf_tensor("table_f", [128, 2, BLOCKS], F32))

        def by_term(scratch, halves):
            v = scratch.rearrange("(m t p) n -> t m p n", m=2, t=TERMS)
            return [(half, v[t]) for t, half in enumerate(halves)]

        def plain(scratch):
            return [(half, scratch[half].rearrange("(m p) n -> m p n", p=128)) for half in range(2)]

        project(nc, "px", a["x_t"], NT // (4 * T), 4 * T,
                [(a["wq_t"], a["bq"], by_term(self_q, (0, 1, 0))), (a["wk_t"], a["bk"], by_term(self_k, (0, 0, 1)))],
                (a["wv_t"], a["bv"], self_v), T)
        project(nc, "pc", a["ctx_t"], B * S // 500, 500,
                [(a["xk_t"], a["xbk"], plain(cross_k))], (a["xv_t"], a["xbv"], cross_v), SC)
        attention(nc, SELF, self_q, self_k, self_v, a["x"], a["wo_t"], a["bo"], x1,
                  wq=a["xq_t"], bq=a["xbq"], q_out=cross_q, w_in=a["experts"], w_out16=w_halves)
        attention(nc, CROSS, cross_k, cross_q, cross_v, x1, a["xo_t"], a["xbo"], x2,
                  gate=a["gate_t"], score_out=scores, lambdas=[a[f"lambda{i}"] for i in range(4)])
        route(nc, scores, x2, routed, table_i, table_f)
        experts(nc, routed, w_halves, table_i, table_f, y)
        finish(nc, x2, y, a["out"])


def kernel(x, ctx_1024, L0_attn_Wq, L0_attn_bq, L0_attn_Wk, L0_attn_bk, L0_attn_Wv, L0_attn_bv, L0_attn_Wo, L0_attn_bo,
           L0_xattn_in_proj_weight, L0_xattn_in_proj_bias, L0_xattn_out_proj_weight, L0_xattn_out_proj_bias,
           L0_xattn_lambda_q1, L0_xattn_lambda_k1, L0_xattn_lambda_q2, L0_xattn_lambda_k2,
           L0_ffn_gate_w, L0_ffn_w1, L0_ffn_w2, L0_ffn_w3):
    import numpy as np
    import concourse.bacc as bacc
    from concourse.bass_utils import run_bass_kernel_spmd

    def cols(b):
        return b.reshape(KD, 128).T

    def units(a):
        lead = a.shape[:-1]
        return np.moveaxis(a.reshape(*lead, PAIRS, 2, DH), -3, -1).reshape(*lead, D)

    w_in, b_in = np.asarray(L0_xattn_in_proj_weight), np.asarray(L0_xattn_in_proj_bias)
    up = [np.asarray(w).transpose(0, 2, 1).reshape(EXP, KD, 128, FF).transpose(0, 2, 1, 3).reshape(EXP, 128, KD * FF)
          for w in (L0_ffn_w1, L0_ffn_w3)]
    down = np.asarray(L0_ffn_w2).transpose(0, 2, 1).reshape(EXP, FC, 128, D).transpose(0, 2, 1, 3).reshape(EXP, 128, FC * D)
    x = np.asarray(x).reshape(NT, D)
    arrays = {
        "x": x,
        "x_t": x.T,
        "ctx_t": np.asarray(ctx_1024).reshape(B * S, D).T,
        "wq_t": units(np.asarray(L0_attn_Wq).T), "bq": cols(units(np.asarray(L0_attn_bq))),
        "wk_t": units(np.asarray(L0_attn_Wk).T), "bk": cols(units(np.asarray(L0_attn_bk))),
        "wv_t": np.asarray(L0_attn_Wv).T, "bv": np.asarray(L0_attn_bv),
        "wo_t": np.asarray(L0_attn_Wo).T, "bo": np.asarray(L0_attn_bo),
        "xq_t": w_in[0:D].T, "xbq": cols(b_in[0:D]),
        "xk_t": w_in[D:2 * D].T, "xbk": cols(b_in[D:2 * D]),
        "xv_t": w_in[2 * D:].T, "xbv": b_in[2 * D:],
        "xo_t": np.asarray(L0_xattn_out_proj_weight).T, "xbo": np.asarray(L0_xattn_out_proj_bias),
        "lambda0": np.asarray(L0_xattn_lambda_q1), "lambda1": np.asarray(L0_xattn_lambda_k1),
        "lambda2": np.asarray(L0_xattn_lambda_q2), "lambda3": np.asarray(L0_xattn_lambda_k2),
        "gate_t": np.asarray(L0_ffn_gate_w).T,
        "experts": np.concatenate(up + [down], axis=2).reshape(EXP, 128, CUTS, CUT).transpose(0, 2, 1, 3).reshape(
            EXP * CUTS, 128, CUT),
    }
    arrays = {f"in_{n}": np.ascontiguousarray(v) for n, v in arrays.items()}
    nc = bacc.Bacc("TRN2", target_bir_lowering=False, num_devices=1)
    a = {n[3:]: nc.dram_tensor(n, v.shape, mybir.dt.from_np(v.dtype), kind="ExternalInput").ap() for n, v in arrays.items()}
    a["out"] = nc.dram_tensor("out_0", (NT, D), F32, kind="ExternalOutput").ap()
    decoder(nc, a)
    got = run_bass_kernel_spmd(nc, [arrays], core_ids=[0]).results[0]["out_0"]
    return got.reshape(B, T, D)
```
